# Optimizing a Trainium2 kernel written in Bass

```python
import numpy as np
import jax
import jax.numpy as jnp

def _softmax(x, axis=-1):
    return jax.nn.softmax(x, axis=axis)

def _gelu(x):
    return jax.nn.gelu(x, approximate=True)

def _silu(x):
    return jax.nn.silu(x)

def _sigmoid(x):
    return jax.nn.sigmoid(x)

def _layernorm(x, axis=-1, eps=1e-05):
    m = jnp.mean(x, axis=axis, keepdims=True)
    v = jnp.var(x, axis=axis, keepdims=True)
    return (x - m) / jnp.sqrt(v + eps)

def _scatter_add(tgt, idx, src, axis=0):
    return tgt.at[idx].add(src)

def _segment_sum(src, seg, n):
    return jax.ops.segment_sum(src, seg, n)
kernel_name = 'mk_xattn_ffn_d1_seqx_r8_f9d2fc'

def setup_inputs(seed: int=0):
    np.random.seed(seed)
    _w = jnp.asarray

    def _rec_inputs():
        import jax
        import jax.numpy as jnp
        _rk = jax.random.key(seed)
        x = 0.002226 + 0.9996 * jax.random.normal(jax.random.fold_in(_rk, 1), (64, 64, 128), jnp.float32)
        _lenS = 64 - jax.random.randint(jax.random.fold_in(_rk, 7), (64,), 0, max(1, 64 // 4) + 1, jnp.int32)
        _lenS2 = 64 - jax.random.randint(jax.random.fold_in(_rk, 8), (64,), 0, max(1, 64 // 4) + 1, jnp.int32)
        _ctx_1024P = jax.random.normal(jax.random.fold_in(_rk, 11), (64, 16, 128), jnp.float32)
        _ctx_1024c = jax.random.dirichlet(jax.random.fold_in(_rk, 511), 0.3 * jnp.ones((16,), jnp.float32), (64, 64))
        _ctx_1024t = jnp.einsum('bsk,bkd->bsd', _ctx_1024c, _ctx_1024P)
        _ctx_1024t = _ctx_1024t * jax.lax.rsqrt(jnp.mean(jnp.square(_ctx_1024t)) + 1e-12) * 0.953939
        ctx_1024 = -7.10856e-05 + 0.999911 * (_ctx_1024t + 0.3 * jax.random.normal(jax.random.fold_in(_rk, 611), (64, 64, 128), jnp.float32))
        return (x, ctx_1024)
    x, ctx_1024 = _rec_inputs()

    def _L0_xattn_setup():
        import jax, jax.numpy as jnp
        import numpy as np
        DIM = 128
        HEAD_DIM = 64
        NUM_HEADS = 8
        INNER = HEAD_DIM * NUM_HEADS
        ROT_DIM = HEAD_DIM
        ROPE_BASE = 10000.0
        EPS = 1e-05

        def layer_norm(x, g, b):
            mu = jnp.mean(x, axis=-1, keepdims=True)
            var = jnp.var(x, axis=-1, keepdims=True)
            return (x - mu) * jax.lax.rsqrt(var + EPS) * g + b

        def rope_rotate_k(k):
            n = k.shape[1]
            half = ROT_DIM // 2
            inv_freq = 1.0 / ROPE_BASE ** (jnp.arange(0, ROT_DIM, 2, dtype=jnp.float32) / ROT_DIM)
            theta = jnp.arange(n, dtype=jnp.float32)[:, None] * inv_freq[None, :]
            angles = jnp.concatenate([theta, theta], axis=-1)
            cos = jnp.cos(angles)[None, :, None, :].astype(k.dtype)
            sin = jnp.sin(angles)[None, :, None, :].astype(k.dtype)
            k_rope, k_pass = (k[..., :ROT_DIM], k[..., ROT_DIM:])
            neg_half = jnp.concatenate([-k_rope[..., half:], k_rope[..., :half]], axis=-1)
            k_rope = k_rope * cos + neg_half * sin
            return jnp.concatenate([k_rope, k_pass], axis=-1)
        key = jax.random.key(seed)
        ks = jax.random.split(key, 5)
        b, n, m = (8, 1024, 64)
        s = 1.0 / np.sqrt(DIM)
        return {'x': jax.random.normal(ks[0], (b, n, DIM), jnp.float32), 'latents': jax.random.normal(ks[1], (b, m, DIM), jnp.float32), 'gamma_x': jnp.ones((DIM,), jnp.float32), 'beta_x': jnp.zeros((DIM,), jnp.float32), 'gamma_l': jnp.ones((DIM,), jnp.float32), 'beta_l': jnp.zeros((DIM,), jnp.float32), 'Wq': jax.random.normal(ks[2], (DIM, INNER), jnp.float32) * s, 'Wkv': jax.random.normal(ks[3], (DIM, 2 * INNER), jnp.float32) * s, 'Wo': jax.random.normal(ks[4], (INNER, DIM), jnp.float32) * (1.0 / np.sqrt(INNER))}
    _L0_xattn_all = _L0_xattn_setup()
    _L0_xattn_in = {k: v for k, v in _L0_xattn_all.items() if k in ('gamma_x', 'beta_x', 'gamma_l', 'beta_l', 'Wq', 'Wkv', 'Wo')}
    del _L0_xattn_all

    def _L0_ffn_setup():
        import jax, jax.numpy as jnp
        import numpy as np
        B, S, H, NH, E, F = (4, 128, 128, 16, 8, 512)
        D = H // NH
        EPS = 1e-05

        def _layernorm(x, g, b):
            mu = jnp.mean(x, axis=-1, keepdims=True)
            var = jnp.var(x, axis=-1, keepdims=True)
            return (x - mu) * jax.lax.rsqrt(var + EPS) * g + b
        key = jax.random.key(seed)
        ks = jax.random.split(key, 16)
        s = 0.02
        return {'x': jax.random.normal(ks[0], (B, S, H), jnp.float32), 'ln1_g': jnp.ones((H,), jnp.float32), 'ln1_b': jnp.zeros((H,), jnp.float32), 'ln2_g': jnp.ones((H,), jnp.float32), 'ln2_b': jnp.zeros((H,), jnp.float32), 'wq': jax.random.normal(ks[1], (H, H), jnp.float32) * s, 'bq': jnp.zeros((H,), jnp.float32), 'wk': jax.random.normal(ks[2], (H, H), jnp.float32) * s, 'bk': jnp.zeros((H,), jnp.float32), 'wv': jax.random.normal(ks[3], (H, H), jnp.float32) * s, 'bv': jnp.zeros((H,), jnp.float32), 'wo': jax.random.normal(ks[4], (H, H), jnp.float32) * s, 'bo': jnp.zeros((H,), jnp.float32), 'gate_w': jax.random.normal(ks[5], (H, E), jnp.float32) * s, 'gate_b': jnp.zeros((E,), jnp.float32), 'w1': jax.random.normal(ks[6], (E, H, F), jnp.float32) * s, 'b1': jnp.zeros((E, F), jnp.float32), 'w2': jax.random.normal(ks[7], (E, F, H), jnp.float32) * s, 'b2': jnp.zeros((E, H), jnp.float32)}
    _L0_ffn_all = _L0_ffn_setup()
    _L0_ffn_in = {k: v for k, v in _L0_ffn_all.items() if k in ('ln1_g', 'ln1_b', 'ln2_g', 'ln2_b', 'wq', 'bq', 'wk', 'bk', 'wv', 'bv', 'wo', 'bo', 'gate_w', 'gate_b', 'w1', 'b1', 'w2', 'b2')}
    del _L0_ffn_all
    return {'x': x, 'ctx_1024': ctx_1024, 'L0_xattn_gamma_x': _L0_xattn_in['gamma_x'], 'L0_xattn_beta_x': _L0_xattn_in['beta_x'], 'L0_xattn_gamma_l': _L0_xattn_in['gamma_l'], 'L0_xattn_beta_l': _L0_xattn_in['beta_l'], 'L0_xattn_Wq': _L0_xattn_in['Wq'], 'L0_xattn_Wkv': _L0_xattn_in['Wkv'], 'L0_xattn_Wo': _L0_xattn_in['Wo'], 'L0_ffn_ln1_g': _L0_ffn_in['ln1_g'], 'L0_ffn_ln1_b': _L0_ffn_in['ln1_b'], 'L0_ffn_ln2_g': _L0_ffn_in['ln2_g'], 'L0_ffn_ln2_b': _L0_ffn_in['ln2_b'], 'L0_ffn_wq': _L0_ffn_in['wq'], 'L0_ffn_bq': _L0_ffn_in['bq'], 'L0_ffn_wk': _L0_ffn_in['wk'], 'L0_ffn_bk': _L0_ffn_in['bk'], 'L0_ffn_wv': _L0_ffn_in['wv'], 'L0_ffn_bv': _L0_ffn_in['bv'], 'L0_ffn_wo': _L0_ffn_in['wo'], 'L0_ffn_bo': _L0_ffn_in['bo'], 'L0_ffn_gate_w': _L0_ffn_in['gate_w'], 'L0_ffn_gate_b': _L0_ffn_in['gate_b'], 'L0_ffn_w1': _L0_ffn_in['w1'], 'L0_ffn_b1': _L0_ffn_in['b1'], 'L0_ffn_w2': _L0_ffn_in['w2'], 'L0_ffn_b2': _L0_ffn_in['b2']}

def reference(x, ctx_1024, L0_xattn_gamma_x, L0_xattn_beta_x, L0_xattn_gamma_l, L0_xattn_beta_l, L0_xattn_Wq, L0_xattn_Wkv, L0_xattn_Wo, L0_ffn_ln1_g, L0_ffn_ln1_b, L0_ffn_ln2_g, L0_ffn_ln2_b, L0_ffn_wq, L0_ffn_bq, L0_ffn_wk, L0_ffn_bk, L0_ffn_wv, L0_ffn_bv, L0_ffn_wo, L0_ffn_bo, L0_ffn_gate_w, L0_ffn_gate_b, L0_ffn_w1, L0_ffn_b1, L0_ffn_w2, L0_ffn_b2):
    import jax
    import jax.numpy as jnp

    def _L0_xattn_ref(x, latents, gamma_x, beta_x, gamma_l, beta_l, Wq, Wkv, Wo):
        import jax, jax.numpy as jnp
        import numpy as np
        DIM = 128
        HEAD_DIM = 64
        NUM_HEADS = 8
        INNER = HEAD_DIM * NUM_HEADS
        ROT_DIM = HEAD_DIM
        ROPE_BASE = 10000.0
        EPS = 1e-05

        def layer_norm(x, g, b):
            mu = jnp.mean(x, axis=-1, keepdims=True)
            var = jnp.var(x, axis=-1, keepdims=True)
            return (x - mu) * jax.lax.rsqrt(var + EPS) * g + b

        def rope_rotate_k(k):
            n = k.shape[1]
            half = ROT_DIM // 2
            inv_freq = 1.0 / ROPE_BASE ** (jnp.arange(0, ROT_DIM, 2, dtype=jnp.float32) / ROT_DIM)
            theta = jnp.arange(n, dtype=jnp.float32)[:, None] * inv_freq[None, :]
            angles = jnp.concatenate([theta, theta], axis=-1)
            cos = jnp.cos(angles)[None, :, None, :].astype(k.dtype)
            sin = jnp.sin(angles)[None, :, None, :].astype(k.dtype)
            k_rope, k_pass = (k[..., :ROT_DIM], k[..., ROT_DIM:])
            neg_half = jnp.concatenate([-k_rope[..., half:], k_rope[..., :half]], axis=-1)
            k_rope = k_rope * cos + neg_half * sin
            return jnp.concatenate([k_rope, k_pass], axis=-1)
        b, n, _ = x.shape
        m = latents.shape[1]
        h, d = (NUM_HEADS, HEAD_DIM)
        scale = d ** (-0.5)
        xn = layer_norm(x, gamma_x, beta_x)
        ln = layer_norm(latents, gamma_l, beta_l)
        q = (ln @ Wq).reshape(b, m, h, d)
        kv_x = xn @ Wkv
        k_x, v_x = (kv_x[..., :INNER], kv_x[..., INNER:])
        kv_l = ln @ Wkv
        k_l, v_l = (kv_l[..., :INNER], kv_l[..., INNER:])
        k_x = k_x.reshape(b, n, h, d)
        v_x = v_x.reshape(b, n, h, d)
        k_x = rope_rotate_k(k_x)
        q = jnp.transpose(q, (0, 2, 1, 3)) * scale
        k_x = jnp.transpose(k_x, (0, 2, 1, 3))
        v_x = jnp.transpose(v_x, (0, 2, 1, 3))
        k_l = jnp.transpose(k_l.reshape(b, m, h, d), (0, 2, 1, 3))
        v_l = jnp.transpose(v_l.reshape(b, m, h, d), (0, 2, 1, 3))
        k = jnp.concatenate([k_x, k_l], axis=2)
        v = jnp.concatenate([v_x, v_l], axis=2)
        sim = jnp.einsum('bhid,bhjd->bhij', q, k)
        attn = jax.nn.softmax(sim, axis=-1)
        out = jnp.einsum('bhij,bhjd->bhid', attn, v)
        out = jnp.transpose(out, (0, 2, 1, 3)).reshape(b, m, INNER)
        return out @ Wo

    def _L0_ffn_ref(x, ln1_g, ln1_b, ln2_g, ln2_b, wq, bq, wk, bk, wv, bv, wo, bo, gate_w, gate_b, w1, b1, w2, b2):
        import jax, jax.numpy as jnp
        import numpy as np
        B, S, H, NH, E, F = (4, 128, 128, 16, 8, 512)
        D = H // NH
        EPS = 1e-05

        def _layernorm(x, g, b):
            mu = jnp.mean(x, axis=-1, keepdims=True)
            var = jnp.var(x, axis=-1, keepdims=True)
            return (x - mu) * jax.lax.rsqrt(var + EPS) * g + b
        b, s, h = x.shape
        hn = _layernorm(x, ln1_g, ln1_b)
        q = (hn @ wq + bq).reshape(b, s, NH, D).transpose(0, 2, 1, 3)
        k = (hn @ wk + bk).reshape(b, s, NH, D).transpose(0, 2, 1, 3)
        v = (hn @ wv + bv).reshape(b, s, NH, D).transpose(0, 2, 1, 3)
        scores = jnp.einsum('bhqd,bhkd->bhqk', q, k) / jnp.sqrt(jnp.float32(D))
        attn = jax.nn.softmax(scores, axis=-1)
        o = jnp.einsum('bhqk,bhkd->bhqd', attn, v)
        o = o.transpose(0, 2, 1, 3).reshape(b, s, h)
        x = x + (o @ wo + bo)
        hn2 = _layernorm(x, ln2_g, ln2_b).reshape(-1, h)
        logits = hn2 @ gate_w + gate_b
        idx = jnp.argmax(logits, axis=-1)
        mid = jax.nn.relu(jnp.einsum('th,ehf->etf', hn2, w1) + b1[:, None, :])
        y = jnp.einsum('etf,efh->eth', mid, w2) + b2[:, None, :]
        moe = y[idx, jnp.arange(hn2.shape[0])]
        return x + moe.reshape(b, s, h)
    x = x + _L0_xattn_ref(ctx_1024, _layernorm(x, axis=-1), L0_xattn_gamma_x, L0_xattn_beta_x, L0_xattn_gamma_l, L0_xattn_beta_l, L0_xattn_Wq, L0_xattn_Wkv, L0_xattn_Wo)
    x = x + _L0_ffn_ref(_layernorm(x, axis=-1), L0_ffn_ln1_g, L0_ffn_ln1_b, L0_ffn_ln2_g, L0_ffn_ln2_b, L0_ffn_wq, L0_ffn_bq, L0_ffn_wk, L0_ffn_bk, L0_ffn_wv, L0_ffn_bv, L0_ffn_wo, L0_ffn_bo, L0_ffn_gate_w, L0_ffn_gate_b, L0_ffn_w1, L0_ffn_b1, L0_ffn_w2, L0_ffn_b2)
    return x

_drawn_inputs = setup_inputs


def setup_inputs(seed=0):
    import zlib

    import numpy as np

    out = dict(_drawn_inputs(seed))
    spreads = {'L0_xattn_gamma_x': (1.0, 0.2),
     'L0_xattn_beta_x': (0.0, 0.1),
     'L0_xattn_gamma_l': (1.0, 0.2),
     'L0_xattn_beta_l': (0.0, 0.1),
     'L0_ffn_ln1_g': (1.0, 0.6),
     'L0_ffn_ln1_b': (0.0, 0.8),
     'L0_ffn_ln2_g': (1.0, 0.2),
     'L0_ffn_ln2_b': (0.0, 0.406),
     'L0_ffn_bq': (0.0, 0.8),
     'L0_ffn_bk': (0.0, 0.8),
     'L0_ffn_bv': (0.0, 0.464),
     'L0_ffn_bo': (0.0, 0.1),
     'L0_ffn_gate_b': (0.0, 0.1),
     'L0_ffn_b1': (0.0, 0.542),
     'L0_ffn_b2': (0.0, 0.1)}
    factors = {'L0_ffn_wq': 8.0, 'L0_ffn_wk': 8.0, 'L0_ffn_wv': 4.866, 'L0_ffn_wo': 3.183}
    for name, (base, spread) in spreads.items():
        noise = np.random.default_rng([zlib.crc32(name.encode()), seed]).standard_normal(out[name].shape)
        drawn = base * np.exp(spread * noise) if base else spread * noise
        out[name] = jnp.asarray(drawn.astype(out[name].dtype))
    for name, factor in factors.items():
        out[name] = (out[name] * factor).astype(out[name].dtype)
    return out
```

```python
from contextlib import ExitStack

import numpy as np

import concourse.bass as bass
from concourse import mybir

F32 = mybir.dt.float32
I32 = mybir.dt.int32
U32 = mybir.dt.uint32
ALU = mybir.AluOpType
ACT = mybir.ActivationFunctionType
AX = mybir.AxisListType

P = 128
B, S, D = 64, 64, 128
XH, XD = 8, 64
PAIRS = XH // 2
FH, FD = 16, 8
QUADS = 4
E, F = 8, 512
FC = F // P
EPS = 1e-5
TILES = B // 2
GB = 4
GROUPS = B // GB
UN = 8
ITER = B // UN
N = B * S
BLOCKS = N // P + E - 1
ROW = 2 * D + 1
NOWHERE = float(1 << 20)
VW = 34

C_ID, C_COS, C_SIN, C_TRI, C_HH = 0, 128, 192, 256, 384
C_E8, C_BLK, C_TOK, C_LNM, C_LNA = 388, 396, 396 + BLOCKS, 397 + BLOCKS, 398 + BLOCKS
C_W = 399 + BLOCKS
R_GX, R_BX, R_GL, R_BL, R_BO, R_G2, R_B2, R_GATE, R_MB2 = 0, 1, 2, 3, 4, 5, 6, 7, 8
R_N = 8 + E
K_G1, K_B1, K_BQ, K_BK, K_BV0, K_BV1, K_G2, K_B2, K_MB1 = range(9)
K_N = K_MB1 + E * FC


def shape_constants():
    c = np.zeros((P, C_W), np.float32)
    p = np.arange(P)
    c[:, C_ID:C_ID + P] = np.eye(P, dtype=np.float32)
    inv = (np.float32(1.0) / np.float32(10000.0) ** (np.arange(0, XD, 2, dtype=np.float32) / np.float32(XD)))
    theta = np.arange(S, dtype=np.float32)[:, None] * inv.astype(np.float32)[None, :]
    d = p % XD
    c[:, C_COS:C_COS + S] = np.cos(theta).astype(np.float32)[:, d % (XD // 2)].T
    sign = np.where(d < XD // 2, -1.0, 1.0).astype(np.float32)
    c[:, C_SIN:C_SIN + S] = sign[:, None] * np.sin(theta).astype(np.float32)[:, d % (XD // 2)].T
    c[:, C_TRI:C_TRI + P] = (p[:, None] < p[None, :]).astype(np.float32)
    c[:, C_HH:C_HH + 4] = ((p // FD) % 4)[:, None] == np.arange(4)[None, :]
    c[:, C_E8:C_E8 + E] = np.arange(E, dtype=np.float32) - E
    c[:, C_BLK:C_BLK + BLOCKS] = np.arange(BLOCKS, dtype=np.float32)
    c[:, C_TOK] = p
    c[:, C_LNM] = np.where(p < 64, 1.0, 1.0 + EPS)
    c[:, C_LNA] = np.where(p < 64, EPS, EPS * EPS)
    return c


def build(nc, kv_rows, x_tiles, consts, rows, cols, proj_w, xo_w, ffn_w, moe_w1, moe_w2, out):
    with ExitStack() as ctx:
        def sb(name, shape, dt=F32):
            return ctx.enter_context(nc.sbuf_tensor(name, shape, dt))

        def psum(name):
            return ctx.enter_context(nc.psum_tensor(name, [P, 512], F32))

        def sem(name):
            return ctx.enter_context(nc.semaphore(name))

        cst = sb("cst", [P, C_W])
        ident = cst[:, C_ID:C_ID + P]
        rowb = sb("rowb", [P, R_N * D])
        colv = sb("colv", [P, K_N])
        lng = sb("lng", [P, D])
        lnb = sb("lnb", [P, D])
        negh = sb("negh", [P, 2 * GB])
        x1 = sb("x1", [P, TILES * D])
        pay = sb("pay", [P, TILES * ROW])
        w1s = sb("w1s", [P, E * F])
        w2s = sb("w2s", [P, E * FC * D])
        pw = sb("pw", [P, 4 * 512])
        wq, wk, wks, wv = (pw[:, n * 512:(n + 1) * 512] for n in range(4))
        xo = sb("xo", [P, PAIRS * D])
        wvT = sb("wvT", [P, PAIRS * P])
        wvo = sb("wvo", [P, XH * D])
        fw = sb("fw", [P, 4 * P + E])
        fwq, fwk, fwv, fwo = (fw[:, n * P:(n + 1) * P] for n in range(4))
        gatew = fw[:, 4 * P:4 * P + E]
        kvraw = [sb(f"kvraw{i}", [P, GB * D]) for i in range(2)]
        kvn = [sb(f"kvn{i}", [P, GB * D]) for i in range(2)]
        kvu = [sb(f"kvu{i}", [P, GB * D]) for i in range(2)]
        kvT = [sb(f"kvT{i}", [P, GB * P]) for i in range(2)]
        qbd = [[sb(f"qbd{i}_{p}", [P, GB * P]) for p in range(PAIRS)] for i in range(2)]
        kk_all = sb("kk_all", [P, 2 * PAIRS * GB * P])
        kk = [[kk_all[:, (PAIRS * i + p) * GB * P:(PAIRS * i + p + 1) * GB * P] for p in range(PAIRS)]
              for i in range(2)]
        rc = [sb(f"rc{i}", [P, GB * S]) for i in range(2)]
        rs = [sb(f"rs{i}", [P, GB * S]) for i in range(2)]
        st6 = sb("st6", [P, GB * 6])
        mv = [sb(f"mv{i}", [P, GB * 2]) for i in range(2)]
        ve = sb("ve", [P, 2 * GB])
        sc = [sb(f"sc{i}", [P, 2 * GB]) for i in range(2)]
        pr = [sb(f"pr{i}", [P, 512]) for i in range(2)]
        prT = [sb(f"prT{i}", [P, 512]) for i in range(2)]
        nmax = [sb(f"nmax{i}", [P, 8]) for i in range(2)]
        esum = [sb(f"esum{i}", [P, 8]) for i in range(2)]
        rsum = [sb(f"rsum{i}", [P, 8]) for i in range(2)]
        uT = [sb(f"uT{i}", [P, XH * P]) for i in range(2)]
        h2z = [kvT[i][:, 0:2 * D] for i in range(2)]
        hnT = [kvT[i][:, 2 * P:4 * P] for i in range(2)]
        qT = [pw[:, i * GB * S:(i + 1) * GB * S] for i in range(2)]
        qh = [sb("qh0", [P, GB * FH * S]), kk_all]
        kT = [pw[:, (2 + i) * GB * S:(3 + i) * GB * S] for i in range(2)]
        vb = [sb(f"vb{i}", [P, GB * QUADS * VW]) for i in range(2)]
        df = kvn
        on = [sb(f"on{i}", [P, S]) for i in range(2)]
        oT = [sb(f"oT{i}", [P, P]) for i in range(2)]
        st6t = sb("st6t", [P, 6])
        mvt = [sb(f"mvt{i}", [P, 2]) for i in range(2)]
        vet = sb("vet", [P, 1])
        sct = [sb(f"sct{i}", [P, 1]) for i in range(2)]
        gT = [sb(f"gT{i}", [P, P]) for i in range(2)]
        hz = [sb(f"hz{i}", [P, D]) for i in range(2)]
        lg = sb("lg", [P, TILES * E])
        def over(t, a, b):
            return t[:, a:b]
        oh = sb("oh", [P, TILES * E])
        ones128 = sb("ones128", [P, P])
        ra = over(qbd[0][0], 0, 256)
        rb = over(qbd[0][0], 256, 512)
        rcnt = over(qbd[0][1], 0, 256)
        rpre = over(qbd[0][1], 256, 512)
        rmx = sb("rmx", [P, TILES])
        sm8 = [sb(f"sm8{i}", [P, E]) for i in range(6)]
        i8 = [sb(f"i8{i}", [P, E], I32) for i in range(2)]
        cmpb = over(kk[1][3], 0, BLOCKS * E)
        eidf = sb("eidf", [P, BLOCKS])
        eid = sb("eid", [P, BLOCKS], I32)
        posf = sb("posf", [P, TILES])
        pos = sb("pos", [P, TILES], U32)
        fillb = sb("fillb", [P, ROW])
        NR = 6
        hr = [over((qbd[1] + kk[1])[i], 0, ROW) for i in range(NR)]
        ids = [sb(f"ids{i}", [P, 1], U32) for i in range(2)]
        hT = [over(qbd[0][2], 128 * i, 128 * i + 128) for i in range(2)]
        yb = [over(qbd[0][3], 128 * i, 128 * i + 128) for i in range(2)]
        ys = [over(qbd[0][3], 256 + 128 * i, 256 + 128 * i + 128) for i in range(2)]
        mid = [kk[0][i] for i in range(2)]
        mT = [kk[0][2 + i] for i in range(2)]

        sorted_rows = nc.dram_tensor("sorted_rows", [BLOCKS * P, ROW], F32).ap()

        bk = [psum(f"bank{i}") for i in range(8)]

        consts_in = sem("consts_in")
        rows_in = sem("rows_in")
        weights_in = sem("weights_in")
        ffn_in = sem("ffn_in")
        moe_in = sem("moe_in")
        x_in = sem("x_in")
        ln_rows = sem("ln_rows")
        zeros_set = sem("zeros_set")
        ones_set = sem("ones_set")
        ones128_set = sem("ones128_set")
        wvT_ready = sem("wvT_ready")
        wvT_copied = sem("wvT_copied")
        wvo_ready = sem("wvo_ready")
        wvo_copied = sem("wvo_copied")
        kv_in = [sem(f"kv_in{i}") for i in range(2)]
        stats_own = sem("stats_own")
        mv_ready = sem("mv_ready")
        ve_own = sem("ve_own")
        sc_ready = sem("sc_ready")
        z_ready = sem("z_ready")
        zg_own = sem("zg_own")
        kvn_ready = sem("kvn_ready")
        kvu_ready = sem("kvu_ready")
        kvT_psum = sem("kvT_psum")
        kvT_ready = sem("kvT_ready")
        qkl_psum = sem("qkl_psum")
        qkl_done = sem("qkl_done")
        kxr_psum = sem("kxr_psum")
        rope_mul = sem("rope_mul")
        rope_done = sem("rope_done")
        s_psum = sem("s_psum")
        max_done = sem("max_done")
        exp_done = sem("exp_done")
        recip_done = sem("recip_done")
        p_norm = sem("p_norm")
        pT_psum = sem("pT_psum")
        pT_done = sem("pT_done")
        u_psum = sem("u_psum")
        u_done = sem("u_done")
        o_psum = sem("o_psum")
        x1_done = sem("x1_done")

        def valid(n, count):
            return not isinstance(n, int) or 0 <= n < count

        def wait(eng, s, value):
            if not isinstance(value, int) or value > 0:
                eng.wait_ge(s, value)

        def apart(eng):
            eng.nop(nofuse=True)

        def pipeline(eng, slot, first=1):
            for i in range(-1, first):
                for j in range(UN):
                    slot(i, j)
            with eng.Fori(first, ITER - 1) as i:
                for j in range(UN):
                    slot(i, j)
            for i in range(ITER - 1, ITER + 1):
                for j in range(UN):
                    slot(i, j)

        def group(t, b, w=D):
            return t[:, b * w:(b + 1) * w]

        a_own = sem("a_own")
        a_mv = sem("a_mv")
        a_ve = sem("a_ve")
        a_ve2 = sem("a_ve2")
        a_sc = sem("a_sc")
        a_z = sem("a_z")
        a_h = sem("a_h")
        a_res = sem("a_res")
        hT_psum = sem("hT_psum")
        hnT_ready = sem("hnT_ready")
        qk_psum = sem("qk_psum")
        qk_done = sem("qk_done")
        v_psum = sem("v_psum")
        v_done = sem("v_done")
        qh_zero = sem("qh_zero")
        qh_in = [sem(f"qh_in{i}") for i in range(2)]
        f_s_psum = sem("f_s_psum")
        f_max = sem("f_max")
        f_sub = sem("f_sub")
        f_exp = sem("f_exp")
        f_pT_psum = sem("f_pT_psum")
        f_pT_done = sem("f_pT_done")
        f_o_psum = sem("f_o_psum")
        f_rec = sem("f_rec")
        f_on = sem("f_on")
        f_onT_psum = sem("f_onT_psum")
        f_oT_done = sem("f_oT_done")
        f_wo_psum = sem("f_wo_psum")
        xf_done = sem("xf_done")
        b_own = sem("b_own")
        b_mv = sem("b_mv")
        b_ve = sem("b_ve")
        b_sc = sem("b_sc")
        b_z = sem("b_z")
        b_g = sem("b_g")
        hn2_ready = sem("hn2_ready")
        res_ready = sem("res_ready")
        gT_psum = sem("gT_psum")
        gT_done = sem("gT_done")
        lg_psum = sem("lg_psum")
        lg_done = sem("lg_done")
        fill_set = sem("fill_set")
        filled = sem("filled")
        tok_set = sem("tok_set")
        route = sem("route")
        oh_ready = sem("oh_ready")
        cnt_psum = sem("cnt_psum")
        pos_ready = sem("pos_ready")
        eid_ready = sem("eid_ready")
        sorted_out = sem("sorted_out")
        hr_in = [sem(f"hr_in{i}") for i in range(NR)]
        m_hT_psum = sem("m_hT_psum")
        m_hT = sem("m_hT")
        m_1_psum = sem("m_1_psum")
        m_mid = sem("m_mid")
        m_T_psum = sem("m_T_psum")
        m_T_act = sem("m_T_act")
        m_T_dve = sem("m_T_dve")
        m_2_psum = sem("m_2_psum")
        m_yb = sem("m_yb")
        m_y = sem("m_y")
        m_ids = sem("m_ids")
        out_sent = [sem(f"out_sent{i}") for i in range(2)]

        bS, bPT, bU, bO, bQ, bK, bX = bk[0:2], bk[2], bk[3], bk[4], bk[5], bk[6], bk[7]

        def t_of(i, j, lag):
            return (UN // 2) * i + (j - lag) // 2

        def payx(t, n):
            v = pay[:, bass.ds(t * ROW, n * ROW)]
            return v.rearrange("p (n w) -> p n w", w=ROW)[:, :, D:2 * D]

        def payh(t):
            return pay[:, bass.ds(t * ROW, D)]

        def expert(eng, n):
            return eng.value_load(eid[0:1, bass.ds(n, 1)], min_val=0, max_val=E - 1)

        def blocks_pipeline(eng, slot):
            for n in range(-2, 4):
                slot(n, n % 2)
            with eng.Fori(2, (BLOCKS - 1) // 2) as i:
                slot(2 * i, 0)
                slot(2 * i + 1, 1)
            for n in range(2 * ((BLOCKS - 1) // 2), BLOCKS + 4):
                slot(n, n % 2)

        block = ctx.enter_context(nc.Block())

        @block.sync
        def _(sp):
            sp.dma_start(cst[:], consts).then_inc(consts_in, 16)

            def load_kv(g, par):
                wait(sp, z_ready, g - 1)
                sp.dma_start(kvraw[par][:], kv_rows[:, bass.ts(g, GB * D)]).then_inc(kv_in[par], 16)

            load_kv(0, 0)
            load_kv(1, 1)
            sp.dma_start(rowb[:], rows.partition_broadcast(P)).then_inc(rows_in, 16)
            sp.dma_start(pw[:], proj_w).then_inc(weights_in, 16)
            sp.dma_start(xo[:], xo_w).then_inc(weights_in, 16)
            load_kv(2, 0)
            load_kv(3, 1)
            sp.dma_start(x1[:], x_tiles).then_inc(x_in, 16)
            sp.dma_start(colv[:], cols).then_inc(ffn_in, 16)
            sp.dma_start(fw[:], ffn_w).then_inc(ffn_in, 16)
            load_kv(4, 0)
            load_kv(5, 1)
            sp.dma_start(w1s[:], moe_w1).then_inc(moe_in, 16)
            sp.dma_start(w2s[:], moe_w2).then_inc(moe_in, 16)
            sp.wait_ge(fill_set, 2)
            for n in range(BLOCKS):
                sp.dma_start(sorted_rows[n * P:(n + 1) * P, :], fillb[:]).then_inc(filled, 16)
            with sp.Fori(3, GROUPS // 2) as i:
                for par in range(2):
                    load_kv(2 * i + par, par)

            sp.wait_ge(qh_zero, 2)

            def spread_heads(g, par):
                sp.wait_ge(qk_done, g + 1)
                apart(sp)
                wait(sp, f_s_psum, GB * (g - 1))
                src = qT[par].rearrange("p (b q) -> p b q", b=GB)
                dst = qh[par].rearrange("p (b h q) -> p b h q", b=GB, h=FH)
                for h in range(FH):
                    pp = slice(FD * h, FD * h + FD)
                    sp.dma_start(dst[pp, :, h, :], src[pp]).then_inc(qh_in[par], 16)

            def slot2(i, j):
                g = 2 * i + j // GB
                if j % GB == 0 and valid(g + 1, GROUPS):
                    spread_heads(g + 1, (j // GB + 1) % 2)

            pipeline(sp, slot2, first=2)

            sp.wait_ge(sorted_out, 16 * TILES)

            def load_rows(n, r):
                wait(sp, m_y, n - NR + 1)
                wait(sp, m_ids, n - NR + 1)
                sp.dma_start(hr[r][:], sorted_rows[bass.ts(n, P), :]).then_inc(hr_in[r], 16)
            for r in range(NR):
                load_rows(r, r)
            with sp.Fori(1, BLOCKS // NR) as i:
                for r in range(NR):
                    load_rows(NR * i + r, r)
            for n in range(NR * (BLOCKS // NR), BLOCKS):
                load_rows(n, n % NR)

        @block.gpsimd
        def _(pool):
            pool.memset(negh[:], -0.5).then_inc(ones_set, 1)
            pool.memset(ones128[:], 1.0).then_inc(ones128_set, 1)
            for i in range(2):
                for p in range(PAIRS):
                    pool.memset(qbd[i][p][:], 0.0)
                pool.memset(vb[i][:], 0.0).then_inc(zeros_set, 1)
            n_set = 2
            for i in range(2):
                v = vb[i].rearrange("p (n w) -> p n w", w=VW)
                for h in range(2):
                    pool.wait_ge(zeros_set, n_set)
                    pool.memset(v[64 * h:64 * h + 64, :, 32 + h:33 + h], 1.0).then_inc(zeros_set, 1)
                    n_set += 1
            pool.wait_ge(zeros_set, n_set)
            pool.memset(fillb[:], 0.0).then_inc(fill_set, 1)
            pool.wait_ge(fill_set, 1)
            pool.memset(fillb[:, 2 * D:ROW], NOWHERE).then_inc(fill_set, 1)
            pool.wait_ge(rows_in, 16)
            for n, (dst, h, r) in enumerate(((lng, 0, R_GX), (lnb, 0, R_BX), (lng, 1, R_GL), (lnb, 1, R_BL))):
                wait(pool, ln_rows, n)
                half = slice(64 * h, 64 * h + 64)
                pool.tensor_copy(dst[half, :], rowb[half, r * D:(r + 1) * D]).then_inc(ln_rows, 1)
            pool.wait_ge(consts_in, 16)
            pool.wait_ge(ones_set, 1)
            pool.wait_ge(ln_rows, 4)

            def ln_scale(g, par):
                pool.wait_ge(mv_ready, g + 1)
                wait(pool, z_ready, g - 1)
                apart(pool)
                var = mv[par].rearrange("p (b two) -> p b two", two=2)[:, :, 1]
                pool.tensor_scalar(ve[:, 0:GB], var, cst[:, C_LNM:C_LNM + 1], cst[:, C_LNA:C_LNA + 1],
                                   ALU.mult, ALU.add).then_inc(ve_own, 1)
                pool.wait_ge(ve_own, g + 1)
                pool.tensor_tensor(sc[par][:, 0:GB], ve[:, 0:GB], negh[:, 0:GB], ALU.pow).then_inc(sc_ready, 1)

            def ln_affine(g, par):
                pool.wait_ge(z_ready, g + 1)
                z = kvn[par].rearrange("p (b d) -> p b d", b=GB)
                pool.tensor_tensor(z, z, lng.rearrange("p (b d) -> p b d", b=1).to_broadcast([P, GB, D]),
                                   ALU.mult).then_inc(zg_own, 1)
                pool.wait_ge(zg_own, g + 1)
                pool.tensor_tensor(z, z, lnb.rearrange("p (b d) -> p b d", b=1).to_broadcast([P, GB, D]),
                                   ALU.add).then_inc(kvn_ready, 1)

            def rope_add(n, g, par, p):
                pool.wait_ge(rope_mul, n + 1)
                if p == 0:
                    wait(pool, s_psum, GB * (g - 1))
                dst = kk[par][p].rearrange("p (b k) -> p b k", b=GB)[:, :, 0:S]
                pool.tensor_tensor(dst, rc[p % 2].rearrange("p (b k) -> p b k", b=GB),
                                   rs[p % 2].rearrange("p (b k) -> p b k", b=GB), ALU.add).then_inc(rope_done, 1)

            def normalise(s, q):
                pool.wait_ge(recip_done, s + 1)
                pv = pr[q].rearrange("p (a k) -> p a k", a=PAIRS)
                pool.tensor_tensor(pv, pv, rsum[q][:, 0:PAIRS].rearrange("p (a k) -> p a k", k=1)
                                   .to_broadcast([P, PAIRS, P]), ALU.mult).then_inc(p_norm, 1)

            def slot(i, j):
                s, g, jj = UN * i + j, 2 * i + j // GB, j % GB
                if jj == 0 and valid(g + 2, GROUPS):
                    ln_scale(g + 2, j // GB)
                if valid(s, B):
                    normalise(s, j % 2)
                if valid(g + 1, GROUPS):
                    rope_add(GB * (g + 1) + jj, g + 1, (j // GB + 1) % 2, jj)
                if jj == 2 and valid(g + 2, GROUPS):
                    ln_affine(g + 2, j // GB)

            pipeline(pool, slot)
            pool.memset(qh[0][:], 0.0).then_inc(qh_zero, 1)
            pool.wait_ge(s_psum, B)
            pool.memset(qh[1][:], 0.0).then_inc(qh_zero, 1)


            def a_scale(g, par):
                pool.wait_ge(a_mv, g + 1)
                wait(pool, a_z, 2 * (g - 1))
                wait(pool, a_h, 2 * (g - 1))
                apart(pool)
                var = mv[par].rearrange("p (b two) -> p b two", two=2)[:, 0:2, 1]
                pool.tensor_scalar(ve[:, 0:2], var, 1.0, EPS, ALU.mult, ALU.add).then_inc(a_ve, 1)
                pool.tensor_scalar(ve[:, 2:4], var, 1.0 + EPS, EPS * EPS, ALU.mult, ALU.add).then_inc(a_ve, 1)
                pool.wait_ge(a_ve, 2 * g + 2)
                pool.tensor_tensor(sc[par][:, 0:4], ve[:, 0:4], negh[:, 0:4], ALU.pow).then_inc(a_sc, 1)

            def a_bias(g):
                pool.wait_ge(a_h, 2 * g + 2)
                hv = payx(2 * g, 2)
                pool.tensor_tensor(hv, hv, rowb[:, R_BO * D:(R_BO + 1) * D].rearrange("p (b d) -> p b d", b=1)
                                   .to_broadcast([P, 2, D]), ALU.add).then_inc(a_res, 1)

            def b_scale(t, par):
                pool.wait_ge(b_mv, t + 1)
                wait(pool, b_z, t - 1)
                apart(pool)
                pool.tensor_scalar(vet[:], mvt[par][:, 1:2], 1.0, EPS, ALU.mult, ALU.add).then_inc(b_ve, 1)
                pool.wait_ge(b_ve, t + 1)
                pool.tensor_tensor(sct[par][:], vet[:], negh[:, 0:1], ALU.pow).then_inc(b_sc, 1)

            def b_affine(t, q):
                pool.wait_ge(b_z, t + 1)
                hv = payh(t)
                apart(pool)
                pool.tensor_tensor(hv, hz[q][:], rowb[:, R_G2 * D:(R_G2 + 1) * D], ALU.mult).then_inc(b_g, 1)
                pool.wait_ge(b_g, t + 1)
                apart(pool)
                pool.tensor_tensor(hv, hv, rowb[:, R_B2 * D:(R_B2 + 1) * D], ALU.add).then_inc(hn2_ready, 1)
                rv = payx(t, 1)[:, 0, :]
                pool.tensor_tensor(rv, rv, x1[:, bass.ts(t, D)], ALU.add).then_inc(res_ready, 1)

            def slot2(i, j):
                s, g, jj, par = UN * i + j, 2 * i + j // GB, j % GB, j // GB
                if jj == 0 and valid(g + 2, GROUPS):
                    a_scale(g + 2, par)
                if jj == 2 and valid(g + 2, GROUPS):
                    a_bias(g + 2)
                if j % 2 == 1 and valid(t_of(i, j, 5), TILES):
                    b_scale(t_of(i, j, 5), ((j - 5) // 2) % 2)
                if j % 2 == 1 and valid(t_of(i, j, 7), TILES):
                    b_affine(t_of(i, j, 7), ((j - 7) // 2) % 2)

            pool.wait_ge(x1_done, TILES)
            pipeline(pool, slot2, first=2)
            pool.wait_ge(b_sc, TILES)

            tokf = pay.rearrange("p (t w) -> p t w", w=ROW)[:, :, 2 * D]
            pool.iota(tokf, pattern=[[P, TILES]], base=0, channel_multiplier=1,
                      allow_small_or_imprecise_dtypes=True).then_inc(tok_set, 1)
            pool.wait_ge(tok_set, 1)
            pool.wait_ge(filled, 16 * BLOCKS)
            pool.wait_ge(res_ready, TILES)
            pool.wait_ge(hn2_ready, TILES)
            pool.wait_ge(pos_ready, 1)
            for t in range(TILES):
                pool.indirect_dma_start(
                    sorted_rows, bass.IndirectOffsetOnAxis(pos[:, t:t + 1], 0), pay[:, t * ROW:(t + 1) * ROW], None,
                ).then_inc(sorted_out, 16)

            for n in range(BLOCKS):
                pool.wait_ge(m_y, n + 1)
                pool.wait_ge(m_ids, n + 1)
                pool.indirect_dma_start(
                    out, bass.IndirectOffsetOnAxis(ids[n % 2][:, 0:1], 0), ys[n % 2], None,
                    bounds_check=N - 1, oob_is_err=False,
                ).then_inc(out_sent[n % 2], 16)
            pool.wait_ge(out_sent[0], 16 * ((BLOCKS + 1) // 2))
            pool.wait_ge(out_sent[1], 16 * (BLOCKS // 2))

        @block.scalar
        def _(act):
            act.wait_ge(wvT_ready, 1)
            act.activation(wvT[:], bS[0][:], ACT.Copy).then_inc(wvT_copied, 1)
            for h in range(2):
                act.wait_ge(wvo_ready, h + 1)
                act.activation(wvo[:, h * 512:(h + 1) * 512], bk[1 + h][:], ACT.Copy).then_inc(wvo_copied, 1)
            act.wait_ge(zeros_set, 6)

            def exps(s, q):
                act.wait_ge(max_done, s + 1)
                wait(act, pT_psum, s - 1)
                wait(act, recip_done, s - 1)
                for p in range(PAIRS):
                    last = act.activation(pr[q][:, p * P:(p + 1) * P], bS[q][:, p * P:(p + 1) * P], ACT.Exp,
                                          bias=nmax[q][:, p:p + 1], accum_out=esum[q][:, p:p + 1])
                last.then_inc(exp_done, 1)

            def queries(n, g, par, p):
                act.wait_ge(qkl_psum, n + 1)
                if p == 0:
                    wait(act, s_psum, GB * (g - 1))
                src = bQ[:, 0:GB * S].rearrange("p (b q) -> p b q", b=GB)
                dst = qbd[par][p].rearrange("p (b h q) -> p b h q", b=GB, h=2)
                for h in range(2):
                    act.activation(dst[64 * h:64 * h + 64, :, h, :], src[64 * h:64 * h + 64], ACT.Copy,
                                   scale=float(XD) ** -0.5)
                act.activation(kk[par][p].rearrange("p (b k) -> p b k", b=GB)[:, :, S:2 * S],
                               bQ[:, GB * S:2 * GB * S].rearrange("p (b q) -> p b q", b=GB),
                               ACT.Copy).then_inc(qkl_done, 1)

            def u_copy(s, i, j):
                act.wait_ge(u_psum, s + 1)
                t = s // 2 if isinstance(s, int) else (UN // 2) * i + (j - 1) // 2
                if j % 2 == 1:
                    wait(act, o_psum, t - 1)
                q = ((j - 1) // 2) % 2
                dst = uT[q].rearrange("p (h b q) -> p h b q", h=XH, b=2)[:, :, (j - 1) % 2, :]
                act.activation(dst, bU[:].rearrange("p (h q) -> p h q", h=XH), ACT.Copy).then_inc(u_done, 1)

            def kvT_copy(g, par):
                act.wait_ge(kvT_psum, g + 1)
                wait(act, qkl_psum, GB * (g - 1))
                wait(act, kxr_psum, GB * (g - 1))
                act.activation(kvT[par][:], bX[:], ACT.Copy).then_inc(kvT_ready, 1)

            def slot(i, j):
                s, g, jj = UN * i + j, 2 * i + j // GB, j % GB
                if valid(s, B):
                    exps(s, j % 2)
                if valid(g + 1, GROUPS):
                    queries(GB * (g + 1) + jj, g + 1, (j // GB + 1) % 2, jj)
                if valid(s - 1, B):
                    u_copy(s - 1, i, j)
                if jj == 3 and valid(g + 2, GROUPS):
                    kvT_copy(g + 2, j // GB)

            pipeline(act, slot)

            act.wait_ge(ffn_in, 32)

            def hnT_copy(g, par):
                act.wait_ge(hT_psum, g + 1)
                wait(act, v_psum, g - 1)
                act.activation(hnT[par], bk[4][:, 0:2 * P], ACT.Identity, scale=colv[:, K_G1:K_G1 + 1],
                               bias=colv[:, K_B1:K_B1 + 1]).then_inc(hnT_ready, 1)

            def v_copy(g, par):
                act.wait_ge(v_psum, g + 1)
                wait(act, f_o_psum, GB * (g - 1))
                src = bk[6][:, 0:2 * P].rearrange("p (c a w) -> p c a w", c=2, w=32)
                dst = vb[par].rearrange("p (c b a w) -> p c b a w", c=2, b=2, w=VW)
                for b in range(2):
                    for h in range(2):
                        last = act.activation(dst[64 * h:64 * h + 64, :, b, :, 16 * h:16 * h + 16],
                                              src[64 * b:64 * b + 64, :, :, 16 * h:16 * h + 16], ACT.Copy)
                last.then_inc(v_done, 1)

            def f_exps(s, q):
                act.wait_ge(f_sub, s + 1)
                wait(act, f_pT_psum, s - 1)
                act.activation(pr[q][:], df[q][:], ACT.Exp, scale=float(FD) ** -0.5).then_inc(f_exp, 1)

            def f_pT(s, q):
                act.wait_ge(f_pT_psum, s + 1)
                wait(act, f_o_psum, s - 1)
                act.activation(prT[q][:], bk[2][:], ACT.Copy).then_inc(f_pT_done, 1)

            def oT_copy(s, i, j):
                act.wait_ge(f_onT_psum, s + 1)
                jb = (j - 3) % 4
                if jb % 2 == 0:
                    wait(act, f_wo_psum, t_of(i, j, 3) - 1)
                for h in range(2):
                    last = act.activation(oT[jb // 2][64 * h:64 * h + 64, S * (jb % 2):S * (jb % 2) + S],
                                          bk[3][0:64, 256 + 64 * h:256 + 64 * h + 64], ACT.Identity,
                                          bias=colv[0:64, K_BV0 + h:K_BV0 + h + 1])
                last.then_inc(f_oT_done, 1)

            def gT_copy(t, q):
                act.wait_ge(gT_psum, t + 1)
                wait(act, lg_psum, t - 1)
                act.activation(gT[q][:], bk[7][:, 256:384], ACT.Identity, scale=colv[:, K_G2:K_G2 + 1],
                               bias=colv[:, K_B2:K_B2 + 1]).then_inc(gT_done, 1)

            def slot2(i, j):
                s, g, jj, par = UN * i + j, 2 * i + j // GB, j % GB, j // GB
                if valid(s - 2, B):
                    f_pT(s - 2, j % 2)
                if valid(s - 3, B):
                    oT_copy(s - 3, i, j)
                if valid(s, B):
                    f_exps(s, j % 2)
                if jj == 1 and valid(g + 1, GROUPS):
                    v_copy(g + 1, (par + 1) % 2)
                if jj == 3 and valid(g + 2, GROUPS):
                    hnT_copy(g + 2, par)
                if j % 2 == 1 and valid(t_of(i, j, 7), TILES):
                    gT_copy(t_of(i, j, 7), ((j - 7) // 2) % 2)

            pipeline(act, slot2, first=2)

            act.wait_ge(eid_ready, 1)

            def mid_copy(n, q):
                act.wait_ge(m_1_psum, n + 1)
                wait(act, m_T_psum, n - 1)
                act.activation(mid[q][:], bk[1 + q][:], ACT.Copy).then_inc(m_mid, 1)

            def relu_half(n, q):
                e = expert(act, n)
                act.wait_ge(m_T_psum, n + 1)
                wait(act, m_2_psum, n - 1)
                for c in (0, 1):
                    last = act.activation(mT[q][:, c * P:(c + 1) * P], bk[3][:, c * P:(c + 1) * P], ACT.Relu,
                                          bias=colv[:, bass.ds(e * FC + (K_MB1 + c), 1)])
                last.then_inc(m_T_act, 1)

            def slot3(n, q):
                if valid(n - 1, BLOCKS):
                    relu_half(n - 1, 1 - q)
                if valid(n, BLOCKS):
                    mid_copy(n, q)
            blocks_pipeline(act, slot3)

        @block.vector
        def _(dve):
            dve.wait_ge(consts_in, 16)

            def ln_stats(g, par):
                dve.wait_ge(kv_in[par], 16 * (half_up(g) + 1))
                wait(dve, mv_ready, g)
                for b in range(GB):
                    last = dve.bn_stats(st6[:, 6 * b:6 * b + 6], group(kvraw[par], b))
                last.then_inc(stats_own, 1)
                dve.wait_ge(stats_own, g + 1)
                wait(dve, sc_ready, g - 1)
                apart(dve)
                for b in range(GB):
                    last = dve.bn_aggr(mv[par][:, 2 * b:2 * b + 2], st6[:, 6 * b:6 * b + 6])
                last.then_inc(mv_ready, 1)

            def half_up(g):
                return g // 2 if isinstance(g, int) else g_half[0]

            g_half = [None]

            def ln_apply(g, par):
                dve.wait_ge(sc_ready, g + 1)
                wait(dve, kvT_psum, g - 1)
                wait(dve, kvu_ready, g - 1)
                for b in range(GB):
                    last = dve.tensor_scalar(group(kvn[par], b), group(kvraw[par], b), mv[par][:, 2 * b:2 * b + 1],
                                             sc[par][:, b:b + 1], ALU.subtract, ALU.mult)
                last.then_inc(z_ready, 1)

            def kvu_copy(g, par):
                dve.wait_ge(kvn_ready, g + 1)
                wait(dve, u_psum, GB * (g - 1))
                dve.tensor_copy(kvu[par][:], kvn[par][:]).then_inc(kvu_ready, 1)

            def row_max(s, q):
                dve.wait_ge(s_psum, s + 1)
                wait(dve, exp_done, s - 1)
                dve.tensor_reduce(nmax[q][:, 0:PAIRS], bS[q][:].rearrange("p (a k) -> p a k", a=PAIRS), AX.X,
                                  ALU.max, negate=True).then_inc(max_done, 1)

            def pT_copy(s, q):
                dve.wait_ge(pT_psum, s + 1)
                wait(dve, u_psum, s - 1)
                dve.tensor_copy(prT[q][:], bPT[:]).then_inc(pT_done, 1)

            def rope(n, p):
                dve.wait_ge(kxr_psum, n + 1)
                wait(dve, rope_done, n - 1)
                for half, dst, tab in ((0, rc, C_COS), (1, rs, C_SIN)):
                    last = dve.tensor_tensor(
                        dst[p % 2].rearrange("p (b k) -> p b k", b=GB),
                        bK[:, half * GB * S:(half + 1) * GB * S].rearrange("p (b k) -> p b k", b=GB),
                        cst[:, tab:tab + S].rearrange("p (b k) -> p b k", b=1).to_broadcast([P, GB, S]), ALU.mult)
                last.then_inc(rope_mul, 1)

            def recip(s, q):
                dve.wait_ge(exp_done, s + 1)
                wait(dve, p_norm, s - 1)
                dve.reciprocal(rsum[q][:, 0:PAIRS], esum[q][:, 0:PAIRS]).then_inc(recip_done, 1)

            def residual(t):
                dve.wait_ge(o_psum, t + 1)
                if isinstance(t, int) and t == 0:
                    dve.wait_ge(x_in, 16)
                xt = x1[:, bass.ts(t, D)]
                dve.tensor_tensor(xt, bO[:, 0:D], xt, ALU.add).then_inc(x1_done, 1)

            def slot(i, j):
                s, g, jj, par = UN * i + j, 2 * i + j // GB, j % GB, j // GB
                g_half[0] = i + 1
                if valid(s, B):
                    row_max(s, j % 2)
                if valid(s - 1, B):
                    pT_copy(s - 1, (j - 1) % 2)
                if jj == 0 and valid(g, GROUPS):
                    kvu_copy(g, par)
                if jj == 0 and valid(g + 2, GROUPS):
                    ln_stats(g + 2, par)
                if jj == 1 and valid(g + 2, GROUPS):
                    ln_apply(g + 2, par)
                if valid(s, B):
                    recip(s, j % 2)
                if valid(g + 1, GROUPS):
                    rope(GB * (g + 1) + jj, jj)
                if j % 2 == 1 and valid(t_of(i, j, 3), TILES):
                    residual(t_of(i, j, 3))

            pipeline(dve, slot)

            dve.wait_ge(ffn_in, 32)
            dve.wait_ge(x1_done, TILES)
            dve.wait_ge(z_ready, GROUPS)

            def a_stats(g, par):
                wait(dve, a_mv, g)
                apart(dve)
                for b in range(2):
                    last = dve.bn_stats(st6[:, 6 * b:6 * b + 6], x1[:, bass.ds(g * (2 * D) + b * D, D)])
                last.then_inc(a_own, 1)
                dve.wait_ge(a_own, g + 1)
                wait(dve, a_sc, g - 1)
                apart(dve)
                for b in range(2):
                    last = dve.bn_aggr(mv[par][:, 2 * b:2 * b + 2], st6[:, 6 * b:6 * b + 6])
                last.then_inc(a_mv, 1)

            def a_apply(g, par):
                dve.wait_ge(a_sc, g + 1)
                wait(dve, hT_psum, g - 1)
                for b in range(2):
                    xt = x1[:, bass.ds(g * (2 * D) + b * D, D)]
                    dve.tensor_scalar(h2z[par][:, b * D:(b + 1) * D], xt, mv[par][:, 2 * b:2 * b + 1],
                                      sc[par][:, 2 + b:3 + b], ALU.subtract, ALU.mult).then_inc(a_z, 1)
                    dve.tensor_scalar(pay[:, bass.ds(g * (2 * ROW) + (b * ROW + D), D)], xt,
                                      mv[par][:, 2 * b:2 * b + 1], sc[par][:, b:b + 1], ALU.subtract,
                                      ALU.mult).then_inc(a_h, 1)

            def qk_copy(g, par):
                dve.wait_ge(qk_psum, g + 1)
                wait(dve, f_s_psum, GB * (g - 1))
                dve.tensor_scalar(qT[par][:], bk[5][:, 0:GB * S], colv[:, K_BQ:K_BQ + 1], None, ALU.add)
                dve.tensor_scalar(kT[par][:], bk[5][:, GB * S:2 * GB * S], colv[:, K_BK:K_BK + 1], None,
                                  ALU.add).then_inc(qk_done, 1)

            def f_row_max(s, q):
                dve.wait_ge(f_s_psum, s + 1)
                sv = bS[q][:].rearrange("p (a k) -> p a k", a=8)
                wait(dve, f_sub, s - 1)
                dve.tensor_reduce(nmax[q][:], sv, AX.X, ALU.max, negate=True).then_inc(f_max, 1)
                dve.wait_ge(f_max, s + 1)
                wait(dve, f_exp, s - 1)
                dve.tensor_tensor(df[q].rearrange("p (a k) -> p a k", a=8), sv,
                                  nmax[q].rearrange("p (a k) -> p a k", k=1).to_broadcast([P, 8, S]),
                                  ALU.add).then_inc(f_sub, 1)

            def f_norm(s, q):
                dve.wait_ge(f_o_psum, s + 1)
                wait(dve, f_on, s - 1)
                ov = bk[3][:, 0:QUADS * VW].rearrange("p (a w) -> p a w", w=VW)
                rv = rsum[q].rearrange("p (a two) -> p a two", two=2)
                dve.reciprocal(rv, ov[:, :, 32:34]).then_inc(f_rec, 1)
                dve.wait_ge(f_rec, s + 1)
                wait(dve, f_onT_psum, s - 1)
                for h in range(2):
                    pp = slice(64 * h, 64 * h + 64)
                    last = dve.tensor_tensor(
                        on[q][pp, :].rearrange("p (a b d) -> p a b d", a=QUADS, b=2),
                        ov[pp, :, 0:32].rearrange("p a (b h d) -> p a b h d", b=2, h=2)[:, :, :, h, :],
                        rsum[q][pp, :].rearrange("p (a b d) -> p a b d", a=QUADS, d=1)
                        .to_broadcast([64, QUADS, 2, FD]), ALU.mult)
                last.then_inc(f_on, 1)

            def xf_add(t):
                dve.wait_ge(f_wo_psum, t + 1)
                if isinstance(t, int):
                    dve.wait_ge(a_res, t // 2 + 1)
                else:
                    dve.wait_ge(a_res, a_need[0])
                xv = payx(t, 1)[:, 0, :]
                dve.tensor_tensor(xv, bk[7][:, 0:D], xv, ALU.add).then_inc(xf_done, 1)

            a_need = [None]

            def b_stats(t, par):
                dve.wait_ge(xf_done, t + 1)
                wait(dve, b_mv, t)
                apart(dve)
                dve.bn_stats(st6t[:], payx(t, 1)[:, 0, :]).then_inc(b_own, 1)
                dve.wait_ge(b_own, t + 1)
                wait(dve, b_sc, t - 1)
                wait(dve, b_z, t - 1)
                apart(dve)
                dve.bn_aggr(mvt[par][:], st6t[:]).then_inc(b_mv, 1)

            def b_apply(t, par):
                dve.wait_ge(b_sc, t + 1)
                wait(dve, gT_psum, t - 1)
                wait(dve, b_g, t - 1)
                dve.tensor_scalar(hz[par][:], payx(t, 1)[:, 0, :], mvt[par][:, 0:1], sct[par][:, 0:1],
                                  ALU.subtract, ALU.mult).then_inc(b_z, 1)

            def lg_copy(t):
                dve.wait_ge(lg_psum, t + 1)
                dve.tensor_tensor(lg[:, bass.ts(t, E)], bk[7][:, 128:128 + E],
                                  rowb[:, R_GATE * D:R_GATE * D + E], ALU.add).then_inc(lg_done, 1)

            def slot2(i, j):
                s, g, jj, par = UN * i + j, 2 * i + j // GB, j % GB, j // GB
                if valid(s, B):
                    f_row_max(s, j % 2)
                if j % 2 == 0 and valid(t_of(i, j, 6), TILES):
                    b_apply(t_of(i, j, 6), ((j - 6) // 2) % 2)
                if j % 2 == 0 and valid(t_of(i, j, 8), TILES):
                    lg_copy(t_of(i, j, 8))
                if j % 2 == 1 and valid(t_of(i, j, 5), TILES):
                    t = t_of(i, j, 5)
                    a_need[0] = 2 * i + (j - 5) // 4 + 1
                    xf_add(t)
                if valid(s - 2, B):
                    f_norm(s - 2, j % 2)
                if jj == 0 and valid(g + 1, GROUPS):
                    qk_copy(g + 1, (par + 1) % 2)
                if j % 2 == 1 and valid(t_of(i, j, 5), TILES):
                    b_stats(t_of(i, j, 5), ((j - 5) // 2) % 2)
                if jj == 0 and valid(g + 2, GROUPS):
                    a_stats(g + 2, par)
                if jj == 2 and valid(g + 2, GROUPS):
                    a_apply(g + 2, par)

            pipeline(dve, slot2, first=2)

            steps = [0]

            def step(ins):
                steps[0] += 1
                ins.then_inc(route, 1)
                dve.wait_ge(route, steps[0])

            def te(t):
                return t.rearrange("p (t e) -> p t e", e=E)

            def over_e(t):
                return t.rearrange("p (t e) -> p t e", e=1).to_broadcast([P, TILES, E])

            def over_t(t):
                return t.rearrange("p (t e) -> p t e", t=1).to_broadcast([P, TILES, E])

            dve.wait_ge(lg_done, TILES)
            step(dve.tensor_reduce(rmx[:], te(lg[:]), AX.X, ALU.max))
            step(dve.tensor_tensor(te(ra), te(lg[:]), over_e(rmx[:]), ALU.is_ge))
            step(dve.tensor_tensor(te(rb), te(ra), over_t(cst[:, C_E8:C_E8 + E]), ALU.mult))
            step(dve.tensor_reduce(rmx[:], te(rb), AX.X, ALU.min))
            dve.tensor_tensor(te(oh[:]), over_t(cst[:, C_E8:C_E8 + E]), over_e(rmx[:]),
                              ALU.is_equal).then_inc(oh_ready, 1)
            dve.wait_ge(cnt_psum, 1)
            step(dve.tensor_copy(rcnt, bk[1][:, 0:TILES * E]))
            step(dve.tensor_copy(rpre, bk[0][:, 0:TILES * E]))
            src, dst, k = rcnt, ra, 1
            while k < TILES:
                dve.tensor_copy(dst[:, 0:k * E], src[:, 0:k * E])
                step(dve.tensor_tensor(dst[:, k * E:], src[:, k * E:], src[:, 0:(TILES - k) * E], ALU.add))
                src, dst, k = dst, (rb if dst is ra else ra), 2 * k
            total = src[:, (TILES - 1) * E:TILES * E]
            step(dve.tensor_scalar(sm8[0][:], total, float(P - 1), None, ALU.add))
            step(dve.tensor_copy(i8[0][:], sm8[0][:]))
            step(dve.tensor_scalar(i8[1][:], i8[0][:], 7, None, ALU.arith_shift_right))
            step(dve.tensor_copy(sm8[1][:], i8[1][:]))
            a, b, k = sm8[1], sm8[2], 1
            while k < E:
                dve.tensor_copy(b[:, 0:k], a[:, 0:k])
                step(dve.tensor_tensor(b[:, k:E], a[:, k:E], a[:, 0:E - k], ALU.add))
                a, b, k = b, (sm8[3] if b is sm8[2] else sm8[2]), 2 * k
            step(dve.tensor_tensor(sm8[4][:], a[:], sm8[1][:], ALU.subtract))
            step(dve.tensor_scalar(sm8[5][:], sm8[4][:], float(P), None, ALU.mult))
            step(dve.tensor_tensor(dst, src, rcnt, ALU.subtract))
            step(dve.tensor_tensor(rpre, rpre, dst, ALU.add))
            step(dve.tensor_tensor(te(rpre), te(rpre), over_t(sm8[5][:]), ALU.add))
            step(dve.tensor_tensor(rpre, rpre, oh[:], ALU.mult))
            step(dve.tensor_reduce(posf[:], te(rpre), AX.X, ALU.add))
            dve.tensor_copy(pos[:], posf[:]).then_inc(pos_ready, 1)
            step(dve.tensor_tensor(cmpb.rearrange("p (n e) -> p n e", e=E),
                                   sm8[4].rearrange("p (n e) -> p n e", n=1).to_broadcast([P, BLOCKS, E]),
                                   cst[:, C_BLK:C_BLK + BLOCKS].rearrange("p (n e) -> p n e", e=1)
                                   .to_broadcast([P, BLOCKS, E]), ALU.is_le))
            step(dve.tensor_reduce(eidf[:], cmpb.rearrange("p (n e) -> p n e", e=E), AX.X, ALU.add))
            step(dve.tensor_scalar(eidf[:], eidf[:], -1.0, None, ALU.add))
            dve.tensor_copy(eid[:], eidf[:]).then_inc(eid_ready, 1)
            dve.wait_ge(eid_ready, 1)

            def hT_copy(n, q):
                dve.wait_ge(m_hT_psum, n + 1)
                wait(dve, m_1_psum, n - 1)
                dve.tensor_copy(hT[q], bk[0][:, 0:P]).then_inc(m_hT, 1)

            def relu_half(n, q, e):
                dve.wait_ge(m_T_psum, n + 1)
                wait(dve, m_2_psum, n - 1)
                for c in (2, 3):
                    last = dve.tensor_scalar(mT[q][:, c * P:(c + 1) * P], bk[4][:, (c - 2) * P:(c - 1) * P],
                                             colv[:, bass.ds(e * FC + (K_MB1 + c), 1)], 0.0, ALU.add, ALU.max)
                last.then_inc(m_T_dve, 1)

            def result(n, q, r, e):
                dve.wait_ge(m_2_psum, n + 1)
                wait(dve, m_y, n - 1)
                dve.tensor_tensor(yb[q], bk[5 + q][:, 0:D], rowb[:, bass.ds(e * D + R_MB2 * D, D)],
                                  ALU.add).then_inc(m_yb, 1)
                dve.wait_ge(m_yb, n + 1)
                sent = n // 2 if isinstance(n, int) else n_half[0]
                wait(dve, out_sent[q], 16 * sent)
                dve.tensor_copy(ids[q][:], hr[r][:, 2 * D:ROW]).then_inc(m_ids, 1)
                dve.tensor_tensor(ys[q], yb[q], hr[r][:, D:2 * D], ALU.add).then_inc(m_y, 1)

            n_half = [None]

            def slot3(n, k):
                e1 = expert(dve, n - 1) if valid(n - 1, BLOCKS) else None
                e2 = expert(dve, n - 2) if valid(n - 2, BLOCKS) else None
                if valid(n - 2, BLOCKS):
                    result(n - 2, k % 2, (k - 2) % NR, e2)
                if valid(n + 1, BLOCKS):
                    hT_copy(n + 1, (k + 1) % 2)
                if valid(n - 1, BLOCKS):
                    relu_half(n - 1, (k - 1) % 2, e1)

            for n in range(-2, NR):
                slot3(n, n % NR)
            with dve.Fori(1, (BLOCKS - 1) // NR) as i:
                for k in range(NR):
                    n_half[0] = 3 * i + (k - 2) // 2
                    slot3(NR * i + k, k)
            for n in range(NR * ((BLOCKS - 1) // NR), BLOCKS + 4):
                slot3(n, n % NR)

        @block.tensor
        def _(pe):
            pe.wait_ge(consts_in, 16)
            pe.wait_ge(weights_in, 32)
            for p in range(PAIRS):
                last = pe.transpose(bS[0][:, p * P:(p + 1) * P], wv[:, p * P:(p + 1) * P], ident)
            last.then_inc(wvT_ready, 1)
            pe.wait_ge(wvT_copied, 1)
            for h in range(2):
                for p in range(PAIRS):
                    last = pe.matmul(bk[1 + h][:, p * D:(p + 1) * D], wvT[64 * h:64 * h + 64, p * P:(p + 1) * P],
                                     xo[64 * h:64 * h + 64, p * D:(p + 1) * D], start=True, stop=True)
                last.then_inc(wvo_ready, 1)
            pe.wait_ge(wvo_copied, 2)

            def kv_transposes(g, par):
                pe.wait_ge(kvn_ready, g + 1)
                wait(pe, kvT_ready, g)
                for b in range(GB):
                    last = pe.transpose(bX[:, b * P:(b + 1) * P], group(kvn[par], b), ident)
                last.then_inc(kvT_psum, 1)

            def project(n, g, par, p):
                if p == 0:
                    pe.wait_ge(kvT_ready, g + 1)
                kv = kvT[par].rearrange("p (b k) -> p b k", b=GB)
                wait(pe, qkl_done, n)
                half = GB * S
                w = slice(p * P, (p + 1) * P)
                pe.matmul(bQ[:, 0:half], wq[:, w], kv[:, :, S:2 * S], start=True, stop=True)
                pe.matmul(bQ[:, half:2 * half], wk[:, w], kv[:, :, S:2 * S], start=True, stop=True).then_inc(qkl_psum, 1)
                wait(pe, rope_mul, n)
                pe.matmul(bK[:, 0:half], wk[:, w], kv[:, :, 0:S], start=True, stop=True)
                pe.matmul(bK[:, half:2 * half], wks[:, w], kv[:, :, 0:S], start=True, stop=True).then_inc(kxr_psum, 1)

            def scores(s, g, par, b, q):
                if b == 0:
                    pe.wait_ge(qkl_done, GB * (g + 1))
                    pe.wait_ge(rope_done, GB * (g + 1))
                wait(pe, exp_done, s - 1)
                for p in range(PAIRS):
                    last = pe.matmul(bS[q][:, p * P:(p + 1) * P], qbd[par][p][:, b * P:(b + 1) * P],
                                     kk[par][p][:, b * P:(b + 1) * P], start=True, stop=True)
                last.then_inc(s_psum, 1)

            def p_transposes(s, q):
                pe.wait_ge(p_norm, s + 1)
                wait(pe, pT_done, s)
                for p in range(PAIRS):
                    last = pe.transpose(bPT[:, p * P:(p + 1) * P], pr[q][:, p * P:(p + 1) * P], ident)
                last.then_inc(pT_psum, 1)

            def values(s, g, par, b, q):
                pe.wait_ge(pT_done, s + 1)
                pe.wait_ge(kvu_ready, g + 1)
                wait(pe, u_done, s)
                pe.matmul(bU[:], group(kvu[par], b), prT[q][:], start=True, stop=True).then_inc(u_psum, 1)

            def outputs(t, q):
                pe.wait_ge(u_done, 2 * t + 2)
                wait(pe, x1_done, t)
                for h in range(XH):
                    col = ((h % 2) * PAIRS + h // 2) * D
                    last = pe.matmul(bO[:, 0:D], uT[q][:, h * P:(h + 1) * P], wvo[:, col:col + D],
                                     start=(h == 0), stop=(h == XH - 1))
                last.then_inc(o_psum, 1)

            def slot(i, j):
                s, g, jj, par = UN * i + j, 2 * i + j // GB, j % GB, j // GB
                if valid(s, B):
                    scores(s, g, par, jj, j % 2)
                if valid(s - 1, B):
                    p_transposes(s - 1, (j - 1) % 2)
                if valid(g + 1, GROUPS):
                    project(GB * (g + 1) + jj, g + 1, (par + 1) % 2, jj)
                if valid(s - 1, B):
                    gp = g if jj else g - 1
                    values(s - 1, gp, par if jj else (par + 1) % 2, (jj - 1) % GB, (j - 1) % 2)
                if j % 2 == 1 and valid(t_of(i, j, 3), TILES):
                    outputs(t_of(i, j, 3), ((j - 3) // 2) % 2)
                if jj == 3 and valid(g + 2, GROUPS):
                    kv_transposes(g + 2, par)

            pipeline(pe, slot)

            pe.wait_ge(ffn_in, 32)
            pe.wait_ge(x1_done, TILES)
            pe.wait_ge(u_done, B)
            pe.wait_ge(zeros_set, 6)

            def h_transposes(g, par):
                pe.wait_ge(a_z, 2 * g + 2)
                wait(pe, hnT_ready, g)
                for b in range(2):
                    last = pe.transpose(bk[4][:, b * P:(b + 1) * P], h2z[par][:, b * D:(b + 1) * D], ident)
                last.then_inc(hT_psum, 1)

            def qk(g, par):
                pe.wait_ge(hnT_ready, g + 1)
                wait(pe, qk_done, g)
                pe.matmul(bk[5][:, 0:GB * S], fwq, hnT[par], start=True, stop=True)
                pe.matmul(bk[5][:, GB * S:2 * GB * S], fwk, hnT[par], start=True, stop=True).then_inc(qk_psum, 1)

            def v(g, par):
                wait(pe, v_done, g)
                for b in range(2):
                    last = pe.matmul(bk[6][:, b * P:(b + 1) * P], hnT[par][:, b * P:(b + 1) * P], fwv,
                                     start=True, stop=True)
                last.then_inc(v_psum, 1)

            def f_scores_wait(s, i, par, b):
                if b == 0:
                    pe.wait_ge(qh_in[par], 16 * FH * (i + 1))
                wait(pe, f_sub, s - 1)

            def f_scores_quad(s, par, b, q, a):
                for k in range(2):
                    n = b * FH + 4 * a + 2 * k
                    last = pe.matmul(bS[q][:, (2 * a + k) * S:(2 * a + k + 1) * S], qh[par][:, n * S:(n + 2) * S],
                                     kT[par][:, b * S:(b + 1) * S], start=True, stop=True)
                if a == QUADS - 1:
                    last.then_inc(f_s_psum, 1)

            def f_transposes_wait(s):
                pe.wait_ge(f_exp, s + 1)
                wait(pe, f_pT_done, s)

            def f_transpose(s, q, a):
                last = pe.transpose(bk[2][:, a * P:(a + 1) * P], pr[q][:, a * P:(a + 1) * P], ident)
                if a == QUADS - 1:
                    last.then_inc(f_pT_psum, 1)

            def f_values(s, g, par, b, q):
                pe.wait_ge(f_pT_done, s + 1)
                pe.wait_ge(v_done, g + 1)
                wait(pe, f_on, s)
                wait(pe, f_oT_done, s)
                for a in range(QUADS):
                    n = b * QUADS + a
                    last = pe.matmul(bk[3][:, a * VW:(a + 1) * VW], prT[q][:, a * P:(a + 1) * P],
                                     vb[par][:, n * VW:(n + 1) * VW], start=True, stop=True)
                last.then_inc(f_o_psum, 1)

            def on_transpose(s, q):
                pe.wait_ge(f_on, s + 1)
                wait(pe, f_oT_done, s)
                apart(pe)
                pe.transpose(bk[3][0:64, 256:384], on[q][:], ident).then_inc(f_onT_psum, 1)

            def wo(t, q):
                pe.wait_ge(f_oT_done, 2 * t + 2)
                wait(pe, xf_done, t)
                wait(pe, lg_done, t - 1)
                pe.matmul(bk[7][:, 0:D], oT[q][:], fwo, start=True, stop=True).then_inc(f_wo_psum, 1)

            def g_transpose(t, q):
                pe.wait_ge(b_z, t + 1)
                if valid(t + 1, TILES):
                    pe.wait_ge(xf_done, t + 2)
                else:
                    pe.wait_ge(lg_done, t)
                wait(pe, gT_done, t)
                pe.transpose(bk[7][:, 256:384], hz[q][:], ident).then_inc(gT_psum, 1)

            def gate(t, q):
                pe.wait_ge(gT_done, t + 1)
                wait(pe, lg_done, t)
                pe.matmul(bk[7][:, 128:128 + E], gT[q][:], gatew, start=True, stop=True).then_inc(lg_psum, 1)

            def slot2(i, j):
                s, g, jj, par = UN * i + j, 2 * i + j // GB, j % GB, j // GB
                if valid(s, B):
                    f_scores_wait(s, i, par, jj)
                for a in range(QUADS):
                    if valid(s, B):
                        f_scores_quad(s, par, jj, j % 2, a)
                    if a == 0 and valid(s - 2, B):
                        f_transposes_wait(s - 2)
                    if valid(s - 2, B):
                        f_transpose(s - 2, j % 2, a)
                if valid(s - 3, B):
                    on_transpose(s - 3, (j - 3) % 2)
                if jj == 0 and valid(g + 1, GROUPS):
                    qk(g + 1, (par + 1) % 2)
                if jj == 1 and valid(g + 1, GROUPS):
                    v(g + 1, (par + 1) % 2)
                if j % 2 == 1 and valid(t_of(i, j, 5), TILES):
                    wo(t_of(i, j, 5), ((j - 5) // 2) % 2)
                if jj == 3 and valid(g + 2, GROUPS):
                    h_transposes(g + 2, par)
                if j % 2 == 0 and valid(t_of(i, j, 8), TILES):
                    gate(t_of(i, j, 8), ((j - 8) // 2) % 2)
                if valid(s - 2, B):
                    old = jj < 2
                    f_values(s - 2, g - 1 if old else g, (par + old) % 2, (jj - 2) % GB, j % 2)
                if j % 2 == 1 and valid(t_of(i, j, 7), TILES):
                    g_transpose(t_of(i, j, 7), ((j - 7) // 2) % 2)

            pipeline(pe, slot2, first=2)

            pe.wait_ge(oh_ready, 1)
            pe.matmul(bk[0][:, 0:TILES * E], cst[:, C_TRI:C_TRI + P], oh[:], start=True, stop=True)
            pe.wait_ge(ones128_set, 1)
            pe.matmul(bk[1][:, 0:TILES * E], ones128[:], oh[:], start=True, stop=True).then_inc(cnt_psum, 1)

            pe.wait_ge(moe_in, 32)
            pe.wait_ge(eid_ready, 1)

            def rows_transpose(n, r):
                pe.wait_ge(hr_in[r], 16 * turn(n))
                wait(pe, m_hT, n)
                pe.transpose(bk[0][:, 0:P], hr[r][:, 0:D], ident).then_inc(m_hT_psum, 1)

            def turn(n):
                return n // NR + 1 if isinstance(n, int) else n_turn[0]

            n_turn = [None]

            def layer1(n, q, e):
                pe.wait_ge(m_hT, n + 1)
                wait(pe, m_mid, n - 1)
                pe.matmul(bk[1 + q][:], hT[q], w1s[:, bass.ds(e * F, F)], start=True, stop=True).then_inc(m_1_psum, 1)

            def mid_transposes(n, q):
                pe.wait_ge(m_mid, n + 1)
                wait(pe, m_T_act, n)
                wait(pe, m_T_dve, n)
                for c in range(FC):
                    last = pe.transpose(bk[3 + c // 2][:, (c % 2) * P:(c % 2 + 1) * P], mid[q][:, c * P:(c + 1) * P], ident)
                last.then_inc(m_T_psum, 1)

            def layer2(n, q, e):
                pe.wait_ge(m_T_act, n + 1)
                pe.wait_ge(m_T_dve, n + 1)
                wait(pe, m_yb, n - 1)
                for c in range(FC):
                    last = pe.matmul(bk[5 + q][:, 0:D], mT[q][:, c * P:(c + 1) * P],
                                     w2s[:, bass.ds(e * (FC * D) + c * D, D)], start=(c == 0), stop=(c == FC - 1))
                last.then_inc(m_2_psum, 1)

            def slot3(n, k):
                e0 = expert(pe, n) if valid(n, BLOCKS) else None
                e1 = expert(pe, n - 1) if valid(n - 1, BLOCKS) else None
                if valid(n + 1, BLOCKS):
                    rows_transpose(n + 1, (k + 1) % NR)
                if valid(n - 1, BLOCKS):
                    mid_transposes(n - 1, (k - 1) % 2)
                if valid(n, BLOCKS):
                    layer1(n, k % 2, e0)
                if valid(n - 1, BLOCKS):
                    layer2(n - 1, (k - 1) % 2, e1)

            for n in range(-2, NR):
                slot3(n, n % NR)
            with pe.Fori(1, (BLOCKS - 1) // NR) as i:
                for k in range(NR):
                    n_turn[0] = i + (k + 1) // NR + 1
                    slot3(NR * i + k, k)
            for n in range(NR * ((BLOCKS - 1) // NR), BLOCKS + 4):
                slot3(n, n % NR)


def kernel(x, ctx_1024, L0_xattn_gamma_x, L0_xattn_beta_x, L0_xattn_gamma_l, L0_xattn_beta_l, L0_xattn_Wq,
           L0_xattn_Wkv, L0_xattn_Wo, L0_ffn_ln1_g, L0_ffn_ln1_b, L0_ffn_ln2_g, L0_ffn_ln2_b, L0_ffn_wq, L0_ffn_bq,
           L0_ffn_wk, L0_ffn_bk, L0_ffn_wv, L0_ffn_bv, L0_ffn_wo, L0_ffn_bo, L0_ffn_gate_w, L0_ffn_gate_b,
           L0_ffn_w1, L0_ffn_b1, L0_ffn_w2, L0_ffn_b2):
    import concourse.bacc as bacc
    from concourse.bass_utils import run_bass_kernel_spmd

    a = np.asarray
    xs, cs = a(x), a(ctx_1024)
    kv_rows = np.concatenate([cs, xs], axis=1).transpose(1, 0, 2).reshape(P, B * D)
    x_tiles = xs.reshape(TILES, P, D).transpose(1, 0, 2).reshape(P, TILES * D)
    wkv = a(L0_xattn_Wkv)
    wk, wv = wkv[:, :512], wkv[:, 512:]
    wks = wk.reshape(D, XH, 2, XD // 2)[:, :, ::-1, :].reshape(D, 512)
    proj_w = np.concatenate([a(L0_xattn_Wq), wk, wks, wv], axis=1)
    xo_w = a(L0_xattn_Wo).reshape(PAIRS, P, D).transpose(1, 0, 2).reshape(P, PAIRS * D)
    gate_row = np.zeros(D, np.float32)
    gate_row[:E] = a(L0_ffn_gate_b)
    rows = np.concatenate([a(L0_xattn_gamma_x), a(L0_xattn_beta_x), a(L0_xattn_gamma_l), a(L0_xattn_beta_l),
                           a(L0_ffn_bo), a(L0_ffn_ln2_g), a(L0_ffn_ln2_b), gate_row, a(L0_ffn_b2).reshape(-1)])
    bv = a(L0_ffn_bv).reshape(FH // 2, 2, FD).transpose(1, 0, 2).reshape(2, 64)
    b1 = a(L0_ffn_b1).reshape(E * FC, P)
    cols = np.stack([a(L0_ffn_ln1_g), a(L0_ffn_ln1_b), a(L0_ffn_bq), a(L0_ffn_bk), bv.reshape(-1),
                     bv[::-1].reshape(-1), a(L0_ffn_ln2_g), a(L0_ffn_ln2_b)] + [b1[n] for n in range(E * FC)], axis=1)
    fwo = a(L0_ffn_wo).reshape(FH // 2, 2, FD, D).transpose(1, 0, 2, 3).reshape(P, D)
    ffn_w = np.concatenate([a(L0_ffn_wq), a(L0_ffn_wk), a(L0_ffn_wv), fwo, a(L0_ffn_gate_w)], axis=1)
    moe_w1 = a(L0_ffn_w1).transpose(1, 0, 2).reshape(P, E * F)
    moe_w2 = a(L0_ffn_w2).reshape(E, FC, P, D).transpose(2, 0, 1, 3).reshape(P, E * FC * D)
    arrays = {"kv_rows": kv_rows, "x_tiles": x_tiles, "consts": shape_constants(), "rows": rows, "cols": cols,
              "proj_w": proj_w, "xo_w": xo_w, "ffn_w": ffn_w, "moe_w1": moe_w1, "moe_w2": moe_w2}
    arrays = {k: np.ascontiguousarray(v) for k, v in arrays.items()}
    nc = bacc.Bacc("TRN2", target_bir_lowering=False, num_devices=1)
    args = {k: nc.dram_tensor(k, v.shape, F32, kind="ExternalInput").ap() for k, v in arrays.items()}
    out = nc.dram_tensor("out", [N, D], F32, kind="ExternalOutput").ap()
    build(nc, out=out, **args)
    r = run_bass_kernel_spmd(nc, [arrays], core_ids=[0])
    return r.results[0]["out"].reshape(B, S, D)
```
